# Optimizing a Trainium2 kernel written in Bass

```python
import numpy as np
import jax
import jax.numpy as jnp

def _softmax(x, axis=-1):
    return jax.nn.softmax(x, axis=axis)

def _gelu(x):
    return jax.nn.gelu(x, approximate=True)

def _silu(x):
    return jax.nn.silu(x)

def _sigmoid(x):
    return jax.nn.sigmoid(x)

def _layernorm(x, axis=-1, eps=1e-05):
    m = jnp.mean(x, axis=axis, keepdims=True)
    v = jnp.var(x, axis=axis, keepdims=True)
    return (x - m) / jnp.sqrt(v + eps)

def _scatter_add(tgt, idx, src, axis=0):
    return tgt.at[idx].add(src)

def _segment_sum(src, seg, n):
    return jax.ops.segment_sum(src, seg, n)
kernel_name = 'mk_rec_standalone_d1_rec_r8_3a3ae0'

def setup_inputs(seed: int=0):
    np.random.seed(seed)
    _w = jnp.asarray

    def _rec_inputs():
        import jax
        import jax.numpy as jnp
        _rk = jax.random.key(seed)
        r_x0 = -9.80646e-05 + 1.00041 * jax.random.normal(jax.random.fold_in(_rk, 1), (2048, 128), jnp.float32)
        r_x = 0.00222621 + 0.99962 * jax.random.normal(jax.random.fold_in(_rk, 2), (2048, 128), jnp.float32)
        return (r_x0, r_x)
    r_x0, r_x = _rec_inputs()

    def _L0_rec_setup():
        import jax, jax.numpy as jnp
        import numpy as np
        B, FIELD, H_PREV, H_NEXT = (512, 128, 128, 256)
        key = jax.random.key(seed)
        k0, k1, k2, k3 = jax.random.split(key, 4)
        x0 = jax.random.normal(k0, (B, FIELD), dtype=jnp.float32)
        x = jax.random.normal(k1, (B, H_PREV), dtype=jnp.float32)
        fan_in = H_PREV * FIELD
        bound = 1.0 / np.sqrt(fan_in)
        W = jax.random.uniform(k2, (H_NEXT, FIELD, H_PREV), dtype=jnp.float32, minval=-bound, maxval=bound)
        b = jax.random.uniform(k3, (H_NEXT,), dtype=jnp.float32, minval=-bound, maxval=bound)
        return {'x0': x0, 'x': x, 'W': W, 'b': b}
    _L0_rec_all = _L0_rec_setup()
    _L0_rec_in = {k: v for k, v in _L0_rec_all.items() if k in ('W', 'b')}
    del _L0_rec_all
    return {'r_x0': r_x0, 'r_x': r_x, 'L0_rec_W': _L0_rec_in['W'], 'L0_rec_b': _L0_rec_in['b']}

def reference(r_x0, r_x, L0_rec_W, L0_rec_b):
    import jax
    import jax.numpy as jnp

    def _L0_rec_ref(x0, x, W, b):
        import jax, jax.numpy as jnp
        import numpy as np
        B, FIELD, H_PREV, H_NEXT = (512, 128, 128, 256)
        outer = x0[:, :, None] * x[:, None, :]
        out = jnp.einsum('bfp,ofp->bo', outer, W) + b
        return out[:, :, None]
    y = _L0_rec_ref(r_x0, r_x, L0_rec_W, L0_rec_b)
    return y

_drawn_inputs = setup_inputs


def setup_inputs(seed=0):
    import zlib

    import numpy as np

    out = dict(_drawn_inputs(seed))
    spreads = {}
    factors = {'L0_rec_b': 7.738}
    for name, (base, spread) in spreads.items():
        noise = np.random.default_rng([zlib.crc32(name.encode()), seed]).standard_normal(out[name].shape)
        drawn = base * np.exp(spread * noise) if base else spread * noise
        out[name] = jnp.asarray(drawn.astype(out[name].dtype))
    for name, factor in factors.items():
        out[name] = (out[name] * factor).astype(out[name].dtype)
    return out
```

```python
import concourse.bass as bass
from concourse import mybir

P = 128
BATCH = 2048
FIELD = 128
H_PREV = 128
H_NEXT = 256
CHUNKS = 8
GROUPS = FIELD * H_PREV // P // CHUNKS
NB = 512
BLOCKS = BATCH // NB
HALVES = H_NEXT // P
PIECE = 4
PIECES = CHUNKS // PIECE
RING = 4
DMA = 16


def chunks_done(g, j):
    return g * CHUNKS + j + 1


def parts_ready(g, j):
    return BLOCKS + g * CHUNKS + j


def splits_ready(g, j):
    return 2 + g * PIECES + j // PIECE


def build(nc, x0_rows, x_rows, w_pieces, bias_cols, out_t):
    f32 = mybir.dt.float32
    f32r = mybir.dt.float32r
    ALU = mybir.AluOpType
    ACT = mybir.ActivationFunctionType

    x_rot = nc.alloc_sbuf_tensor("x_rot", [P, CHUNKS, BATCH], f32)
    x0_rot = nc.alloc_sbuf_tensor("x0_rot", [P, 2, BATCH], f32)
    w_raw = nc.alloc_sbuf_tensor("w_raw", [P, PIECES, PIECE, H_NEXT], f32)
    wh = nc.alloc_sbuf_tensor("wh", [P, PIECES, PIECE, H_NEXT], f32r)
    wl = nc.alloc_sbuf_tensor("wl", [P, PIECES, PIECE, H_NEXT], f32r)
    z = nc.alloc_sbuf_tensor("z", [P, 2, BATCH], f32)
    zh = nc.alloc_sbuf_tensor("zh", [P, RING, BATCH], f32r)
    zl = nc.alloc_sbuf_tensor("zl", [P, RING, BATCH], f32r)
    bias = nc.alloc_sbuf_tensor("bias", [P, HALVES], f32)
    out_sb = nc.alloc_sbuf_tensor("out_sb", [P, HALVES, BATCH], f32)
    acc = nc.alloc_psum_tensor("acc", [P, HALVES, BATCH], f32)

    first_w_loaded = nc.alloc_semaphore("first_w_loaded")
    first_blocks_loaded = [nc.alloc_semaphore(f"first_block{n}_loaded") for n in range(BLOCKS)]
    x_loaded = [nc.alloc_semaphore(f"x_rot{j}_loaded") for j in range(1, CHUNKS)]
    x0_loaded = [nc.alloc_semaphore(f"x0_slot{s}_loaded") for s in range(2)]
    w_loaded = [nc.alloc_semaphore(f"w_slot{s}_loaded") for s in range(PIECES)]
    bias_loaded = nc.alloc_semaphore("bias_loaded")
    z_ready = nc.alloc_semaphore("z_ready")
    zh_ready = nc.alloc_semaphore("zh_ready")
    zl_ready = nc.alloc_semaphore("zl_ready")
    wh_ready = nc.alloc_semaphore("wh_ready")
    wl_ready = nc.alloc_semaphore("wl_ready")
    chunk_multiplied = nc.alloc_semaphore("chunk_multiplied")
    bank_done = nc.alloc_semaphore("bank_done")
    act_bank_copied = nc.alloc_semaphore("act_bank_copied")
    dve_bank_copied = nc.alloc_semaphore("dve_bank_copied")
    out_stored = nc.alloc_semaphore("out_stored")

    with nc.Block() as block:

        def cols(n):
            return slice(n * NB, (n + 1) * NB)

        banks = [(h, n) for n in range(BLOCKS) for h in range(HALVES)]

        @block.sync
        def _(sync):
            def load_x0(g, slot):
                sync.dma_start(x0_rot[:, slot, :], x0_rows[bass.ds(g * CHUNKS, P), :]).then_inc(
                    x0_loaded[slot], DMA)

            def load_w(g, slot):
                sync.dma_start(w_raw[:, slot], w_pieces[bass.ds(g * PIECES + slot, 1)].rearrange(
                    "a k j o -> k (a j) o")).then_inc(w_loaded[slot], DMA)

            sync.dma_start(w_raw[:, 0, 0:1], w_pieces[0, :, 0:1]).then_inc(first_w_loaded, DMA)
            for n in range(BLOCKS):
                sync.dma_start(x0_rot[:, 0, cols(n)], x0_rows[0:P, cols(n)]).then_inc(
                    first_blocks_loaded[n], DMA)
                sync.dma_start(x_rot[:, 0, cols(n)], x_rows[0:P, cols(n)]).then_inc(
                    first_blocks_loaded[n], DMA)
                if n == 0:
                    sync.dma_start(w_raw[:, 0, 1:PIECE], w_pieces[0, :, 1:PIECE]).then_inc(w_loaded[0], DMA)
            for j in range(1, CHUNKS):
                sync.dma_start(x_rot[:, j, :], x_rows[j:j + P, :]).then_inc(x_loaded[j - 1], DMA)
                if j == 2:
                    load_w(0, 1)
            load_x0(1, 1)
            sync.dma_start(bias[:], bias_cols[:, :]).then_inc(bias_loaded, DMA)

            def load_group(g):
                for slot in range(PIECES):
                    sync.wait_ge(wl_ready, splits_ready(g - 1, slot * PIECE))
                    load_w(g, slot)

            def load_next_x0(g, slot):
                sync.wait_ge(z_ready, parts_ready(g - 2, CHUNKS - 1))
                load_x0(g, slot)

            with sync.Fori(1, GROUPS - 1, 2) as g:
                load_group(g)
                load_next_x0(g + 1, 0)
                load_group(g + 1)
                load_next_x0(g + 2, 1)
            load_group(GROUPS - 1)

            for i, (h, n) in enumerate(banks):
                if i % 2 == 0:
                    sync.wait_ge(act_bank_copied, i // 2 + 1)
                else:
                    sync.wait_ge(dve_bank_copied, i // 2 + 1)
                sync.dma_start(out_t[h, :, cols(n)], out_sb[:, h, cols(n)]).then_inc(out_stored, DMA)
            sync.wait_ge(out_stored, DMA * len(banks))

        @block.scalar
        def _(act):
            def round_w(j0, j1, slot):
                nc.scalar.copy(wh[:, slot, j0:j1], w_raw[:, slot, j0:j1]).then_inc(wh_ready, 1)

            def round_z(g, j, first):
                act.wait_ge(z_ready, parts_ready(g, j))
                if not first or j >= RING:
                    act.wait_ge(chunk_multiplied, chunks_done(g, j - RING))
                nc.scalar.copy(zh[:, j % RING, :], z[:, j % 2, :]).then_inc(zh_ready, 1)

            def next_wh(g, j):
                slot = (j + 1) // PIECE % PIECES
                act.wait_ge(w_loaded[slot], DMA * (g + 1 + (j + 1) // CHUNKS))
                act.wait_ge(chunk_multiplied, chunks_done(g, j - PIECE))
                round_w(0, PIECE, slot)

            def group(g):
                for j in range(CHUNKS):
                    round_z(g, j, False)
                    if j % PIECE == PIECE - 1:
                        next_wh(g, j)

            act.wait_ge(first_w_loaded, DMA)
            round_w(0, 1, 0)
            for n in range(BLOCKS):
                act.wait_ge(z_ready, n + 1)
                nc.scalar.copy(zh[:, 0, cols(n)], z[:, 0, cols(n)]).then_inc(zh_ready, 1)
            act.wait_ge(w_loaded[0], DMA)
            round_w(1, PIECE, 0)
            for j in range(1, CHUNKS):
                round_z(0, j, True)
                if j == PIECE - 1:
                    act.wait_ge(w_loaded[1], DMA)
                    round_w(0, PIECE, 1)
            next_wh(0, CHUNKS - 1)
            with act.Fori(1, GROUPS - 1, 2) as g:
                group(g)
                group(g + 1)
            for j in range(CHUNKS):
                round_z(GROUPS - 1, j, False)
                if j == PIECE - 1:
                    next_wh(GROUPS - 1, j)

            act.wait_ge(bias_loaded, DMA)
            for i in range(0, len(banks), 2):
                h, n = banks[i]
                act.wait_ge(bank_done, i + 1)
                nc.scalar.activation(out_sb[:, h, cols(n)], acc[:, h, cols(n)], ACT.Identity,
                                     bias=bias[:, h:h + 1]).then_inc(act_bank_copied, 1)

        @block.vector
        def _(dve):
            def outer_product(j, slot):
                nc.vector.tensor_tensor(z[:, j % 2, :], x0_rot[:, slot, :], x_rot[:, j, :],
                                        ALU.mult).then_inc(z_ready, 1)

            def z_rest(g, j, first):
                dve.wait_ge(zh_ready, parts_ready(g, j))
                if not first or j >= RING:
                    dve.wait_ge(chunk_multiplied, chunks_done(g, j - RING))
                nc.vector.tensor_tensor(zl[:, j % RING, :], z[:, j % 2, :],
                                        zh[:, j % RING, :].bitcast(f32), ALU.subtract).then_inc(zl_ready, 1)

            def w_rest(j0, j1, slot):
                nc.vector.tensor_tensor(wl[:, slot, j0:j1], w_raw[:, slot, j0:j1],
                                        wh[:, slot, j0:j1].bitcast(f32), ALU.subtract).then_inc(wl_ready, 1)

            def next_wl(g, j):
                dve.wait_ge(wh_ready, splits_ready(g, j + 1))
                w_rest(0, PIECE, (j + 1) // PIECE % PIECES)

            def group(g, slot, x0_loads):
                for j in range(CHUNKS):
                    dve.wait_ge(zl_ready, parts_ready(g, j - 1))
                    if j < CHUNKS - 1:
                        outer_product(j + 1, slot)
                    else:
                        dve.wait_ge(x0_loaded[1 - slot], DMA * x0_loads)
                        outer_product(0, 1 - slot)
                    z_rest(g, j, False)
                    if j % PIECE == PIECE - 1:
                        next_wl(g, j)

            for n in range(BLOCKS):
                dve.wait_ge(first_blocks_loaded[n], 2 * DMA)
                nc.vector.tensor_tensor(z[:, 0, cols(n)], x0_rot[:, 0, cols(n)], x_rot[:, 0, cols(n)],
                                        ALU.mult).then_inc(z_ready, 1)
                if n == 0:
                    dve.wait_ge(wh_ready, 1)
                    w_rest(0, 1, 0)
                dve.wait_ge(zh_ready, n + 1)
                nc.vector.tensor_tensor(zl[:, 0, cols(n)], z[:, 0, cols(n)], zh[:, 0, cols(n)].bitcast(f32),
                                        ALU.subtract).then_inc(zl_ready, 1)
            dve.wait_ge(wh_ready, 2)
            w_rest(1, PIECE, 0)
            dve.wait_ge(x_loaded[0], DMA)
            outer_product(1, 0)
            for j in range(1, CHUNKS):
                dve.wait_ge(zl_ready, parts_ready(0, j - 1))
                if j < CHUNKS - 1:
                    dve.wait_ge(x_loaded[j], DMA)
                    outer_product(j + 1, 0)
                else:
                    dve.wait_ge(x0_loaded[1], DMA)
                    outer_product(0, 1)
                z_rest(0, j, True)
                if j % PIECE == PIECE - 1:
                    next_wl(0, j)
            with dve.Fori(1, GROUPS - 1, 2) as g:
                group(g, 1, (g + 1) // 2)
                group(g + 1, 0, (g + 3) // 2)
            for j in range(CHUNKS):
                if j < CHUNKS - 1:
                    dve.wait_ge(zl_ready, parts_ready(GROUPS - 1, j - 1))
                    outer_product(j + 1, 1)
                z_rest(GROUPS - 1, j, False)
                if j == PIECE - 1:
                    next_wl(GROUPS - 1, j)

            dve.wait_ge(bias_loaded, DMA)
            for i in range(1, len(banks), 2):
                h, n = banks[i]
                dve.wait_ge(bank_done, i + 1)
                nc.vector.tensor_scalar(out_sb[:, h, cols(n)], acc[:, h, cols(n)], bias[:, h:h + 1], None,
                                        ALU.add).then_inc(dve_bank_copied, 1)

        @block.tensor
        def _(pe):
            def product(w, zz, j, h, n, start=False, stop=False):
                wj = w[:, j // PIECE, j % PIECE, h * P:(h + 1) * P]
                return nc.tensor.matmul(acc[:, h, cols(n)], wj, zz[:, j % RING, cols(n)],
                                        start=start, stop=stop)

            def chunk(g, j, first_piece_rest=False):
                if j % PIECE == 0 or first_piece_rest:
                    pe.wait_ge(wl_ready, splits_ready(g, j))
                pe.wait_ge(zh_ready, parts_ready(g, j))
                for h in range(HALVES):
                    for n in range(BLOCKS):
                        product(wh, zh, j, h, n)
                    if h == 0:
                        pe.wait_ge(zl_ready, parts_ready(g, j))
                    for n in range(BLOCKS):
                        product(wh, zl, j, h, n)
                    for n in range(BLOCKS):
                        done = product(wl, zh, j, h, n)
                done.then_inc(chunk_multiplied, 1)

            for n in range(BLOCKS):
                pe.wait_ge(wh_ready, 1)
                pe.wait_ge(zh_ready, n + 1)
                for h in range(HALVES):
                    product(wh, zh, 0, h, n, start=True)
                pe.wait_ge(wl_ready, 1)
                for h in range(HALVES):
                    product(wl, zh, 0, h, n)
                pe.wait_ge(zl_ready, n + 1)
                for h in range(HALVES):
                    done = product(wh, zl, 0, h, n)
            done.then_inc(chunk_multiplied, 1)
            for j in range(1, CHUNKS):
                chunk(0, j, first_piece_rest=(j == 1))
            with pe.Fori(1, GROUPS - 1, 2) as g:
                for j in range(CHUNKS):
                    chunk(g, j)
                for j in range(CHUNKS):
                    chunk(g + 1, j)
            for j in range(CHUNKS - 1):
                chunk(GROUPS - 1, j)
            pe.wait_ge(zl_ready, parts_ready(GROUPS - 1, CHUNKS - 1))
            for h, n in banks:
                product(wh, zh, CHUNKS - 1, h, n)
                product(wl, zh, CHUNKS - 1, h, n)
                product(wh, zl, CHUNKS - 1, h, n, stop=True).then_inc(bank_done, 1)


def kernel(r_x0, r_x, L0_rec_W, L0_rec_b):
    import numpy as np
    import concourse.bacc as bacc
    from concourse.bass_utils import run_bass_kernel_spmd

    x0_rows = np.ascontiguousarray(np.concatenate([r_x0.T, r_x0.T]))
    x_rows = np.ascontiguousarray(np.concatenate([r_x.T, r_x.T]))
    k = np.arange(P)
    f = (k[None, :] + CHUNKS * np.arange(GROUPS)[:, None]) % FIELD
    p = (k[None, :] + np.arange(CHUNKS)[:, None]) % H_PREV
    w_by_pair = np.ascontiguousarray(np.asarray(L0_rec_W).transpose(1, 2, 0))
    w_diag = w_by_pair[f[:, None, :], p[None, :, :]]
    w_pieces = np.ascontiguousarray(
        w_diag.reshape(GROUPS * PIECES, PIECE, P, H_NEXT).transpose(0, 2, 1, 3))
    bias_cols = np.ascontiguousarray(np.asarray(L0_rec_b).reshape(HALVES, P).T)

    nc = bacc.Bacc("TRN2", target_bir_lowering=False, num_devices=1)
    arrays = {"x0_rows": x0_rows, "x_rows": x_rows, "w_pieces": w_pieces, "bias_cols": bias_cols}
    args = [nc.dram_tensor(name, a.shape, mybir.dt.from_np(a.dtype), kind="ExternalInput").ap()
            for name, a in arrays.items()]
    out = nc.dram_tensor("out_t", (HALVES, P, BATCH), mybir.dt.float32, kind="ExternalOutput").ap()
    build(nc, *args, out)
    result = run_bass_kernel_spmd(nc, [arrays], core_ids=[0]).results[0]["out_t"]
    return np.ascontiguousarray(result.reshape(H_NEXT, BATCH).T)[:, :, None]
```

```python
import concourse.bass as bass
from concourse import mybir

P = 128
BATCH = 2048
FIELD = 128
H_PREV = 128
H_NEXT = 256
CHUNKS = 8
GROUPS = FIELD * H_PREV // P // CHUNKS
NB = 512
BLOCKS = BATCH // NB
HALVES = H_NEXT // P
PIECE = 4
PIECES = CHUNKS // PIECE
RING = 4
DMA = 16


HALF = BATCH // 2
UNITS = ([(j, 0, NB) for j in range(PIECE)]
         + [(j, NB, HALF) for j in range(PIECE)]
         + [(j, HALF, BATCH) for j in range(PIECE)]
         + [(j, 0, HALF) for j in range(PIECE, CHUNKS)]
         + [(j, HALF, BATCH) for j in range(PIECE, CHUNKS)])
FIRST_STEPS = [(0, 1), (1, 2), (2, PIECE)]
SECOND_PIECE = 3 * PIECE
SPLIT_SECOND = SECOND_PIECE - 3
WARM_UP = 10


def steps_done(g, j):
    return len(UNITS) + (g - 1) * CHUNKS + j + 1


def splits_ready(g, j):
    return len(FIRST_STEPS) + g * PIECES + j // PIECE


def slot_free(u):
    return u - 2 * PIECE + 1 if u >= SECOND_PIECE else 0


def build(nc, x0_rows, x_rows, w_pieces, bias_cols, out_t):
    f32 = mybir.dt.float32
    f32r = mybir.dt.float32r
    ALU = mybir.AluOpType
    ACT = mybir.ActivationFunctionType

    x_rot = nc.alloc_sbuf_tensor("x_rot", [P, CHUNKS, BATCH], f32)
    x0_rot = nc.alloc_sbuf_tensor("x0_rot", [P, 2, BATCH], f32)
    w_raw = nc.alloc_sbuf_tensor("w_raw", [P, PIECES, PIECE, H_NEXT], f32)
    wh = nc.alloc_sbuf_tensor("wh", [P, PIECES, PIECE, H_NEXT], f32r)
    wl = nc.alloc_sbuf_tensor("wl", [P, PIECES, PIECE, H_NEXT], f32r)
    z = nc.alloc_sbuf_tensor("z", [P, RING, BATCH], f32)
    zh = nc.alloc_sbuf_tensor("zh", [P, RING, BATCH], f32r)
    zl = nc.alloc_sbuf_tensor("zl", [P, RING, BATCH], f32r)
    bias = nc.alloc_sbuf_tensor("bias", [P, HALVES], f32)
    out_sb = x_rot[:, 0:HALVES, :]
    zeros = nc.alloc_sbuf_tensor("zeros", [P, NB], mybir.dt.bfloat16)
    acc = nc.alloc_psum_tensor("acc", [P, HALVES, BATCH], f32)

    first_w_loaded = [nc.alloc_semaphore(f"first_w{i}_loaded") for i in range(len(FIRST_STEPS))]
    unit_loaded = [nc.alloc_semaphore(f"unit{u}_loaded") for u in range(len(UNITS))]
    unit_loads = [2 if j == 0 else 1 for j, _, _ in UNITS]
    x0_loaded = [nc.alloc_semaphore(f"x0_slot{s}_loaded") for s in range(2)]
    w_loaded = [nc.alloc_semaphore(f"w_slot{s}_loaded") for s in range(PIECES)]
    zeros_ready = nc.alloc_semaphore("zeros_ready")
    bias_loaded = nc.alloc_semaphore("bias_loaded")
    z_ready = nc.alloc_semaphore("z_ready")
    zh_ready = nc.alloc_semaphore("zh_ready")
    zl_ready = nc.alloc_semaphore("zl_ready")
    wh_ready = nc.alloc_semaphore("wh_ready")
    wl_ready = nc.alloc_semaphore("wl_ready")
    chunk_multiplied = nc.alloc_semaphore("chunk_multiplied")
    bank_done = nc.alloc_semaphore("bank_done")
    act_bank_copied = nc.alloc_semaphore("act_bank_copied")
    dve_bank_copied = nc.alloc_semaphore("dve_bank_copied")
    out_stored = nc.alloc_semaphore("out_stored")

    with nc.Block() as block:

        def cols(n):
            return slice(n * NB, (n + 1) * NB)

        banks = [(h, n) for n in range(BLOCKS) for h in range(HALVES)]
        act_banks = range(0, len(banks), 2)
        dve_banks = range(1, len(banks), 2)

        @block.sync
        def _(sync):
            def load_x0(g, slot):
                sync.dma_start(x0_rot[:, slot, :], x0_rows[bass.ds(g * CHUNKS, P), :]).then_inc(
                    x0_loaded[slot], DMA)

            def load_w(g, slot):
                sync.dma_start(w_raw[:, slot], w_pieces[bass.ds(g * PIECES + slot, 1)].rearrange(
                    "a k j o -> k (a j) o")).then_inc(w_loaded[slot], DMA)

            for u, (j, first, last) in enumerate(UNITS):
                if j == 0:
                    sync.dma_start(x0_rot[:, 0, first:last], x0_rows[0:P, first:last]).then_inc(
                        unit_loaded[u], DMA)
                sync.dma_start(x_rot[:, j, first:last], x_rows[j:j + P, first:last]).then_inc(
                    unit_loaded[u], DMA)
                if u < len(FIRST_STEPS):
                    j0, j1 = FIRST_STEPS[u]
                    sync.dma_start(w_raw[:, 0, j0:j1], w_pieces[0, :, j0:j1]).then_inc(first_w_loaded[u], DMA)
                if u == 2 * PIECE:
                    load_w(0, 1)
            load_x0(1, 1)
            sync.dma_start(bias[:], bias_cols[:, :]).then_inc(bias_loaded, DMA)

            def load_group(g):
                for slot in range(PIECES):
                    sync.wait_ge(wl_ready, splits_ready(g - 1, slot * PIECE))
                    load_w(g, slot)

            def load_next_x0(g, slot):
                sync.wait_ge(z_ready, steps_done(g - 2, CHUNKS - 1))
                load_x0(g, slot)

            with sync.Fori(1, GROUPS - 1, 2) as g:
                load_group(g)
                load_next_x0(g + 1, 0)
                load_group(g + 1)
                load_next_x0(g + 2, 1)
            load_group(GROUPS - 1)

            for copied, i in enumerate(dve_banks):
                h, n = banks[i]
                sync.wait_ge(dve_bank_copied, copied + 1)
                sync.dma_start(out_t[h, :, cols(n)], out_sb[:, h, cols(n)]).then_inc(out_stored, DMA)
            sync.wait_ge(out_stored, DMA * len(banks))

        @block.scalar
        def _(act):
            def round_w(j0, j1, slot):
                nc.scalar.copy(wh[:, slot, j0:j1], w_raw[:, slot, j0:j1]).then_inc(wh_ready, 1)

            def round_z(g, j):
                act.wait_ge(z_ready, steps_done(g, j))
                act.wait_ge(chunk_multiplied, steps_done(g, j - RING))
                nc.scalar.copy(zh[:, j % RING, :], z[:, j % RING, :]).then_inc(zh_ready, 1)

            def next_wh(g, j):
                slot = (j + 1) // PIECE % PIECES
                act.wait_ge(w_loaded[slot], DMA * (g + 1))
                act.wait_ge(chunk_multiplied, steps_done(g, j - PIECE))
                round_w(0, PIECE, slot)

            def group(g):
                for j in range(CHUNKS):
                    round_z(g, j)
                    if j % PIECE == PIECE - 1:
                        next_wh(g, j)

            for u, (j, first, last) in enumerate(UNITS):
                if u < len(FIRST_STEPS):
                    act.wait_ge(first_w_loaded[u], DMA)
                    round_w(*FIRST_STEPS[u], 0)
                act.wait_ge(z_ready, u + 1)
                if slot_free(u):
                    act.wait_ge(chunk_multiplied, slot_free(u))
                nc.scalar.copy(zh[:, j % RING, first:last], z[:, j % RING, first:last]).then_inc(zh_ready, 1)
                if u == SPLIT_SECOND:
                    act.wait_ge(w_loaded[1], DMA)
                    round_w(0, PIECE, 1)
            act.wait_ge(w_loaded[0], DMA)
            act.wait_ge(chunk_multiplied, SECOND_PIECE)
            round_w(0, PIECE, 0)
            with act.Fori(1, GROUPS - 1, 2) as g:
                group(g)
                group(g + 1)
            for j in range(CHUNKS):
                round_z(GROUPS - 1, j)
                if j == PIECE - 1:
                    next_wh(GROUPS - 1, j)

            act.wait_ge(bias_loaded, DMA)
            for copied, i in enumerate(act_banks):
                h, n = banks[i]
                act.wait_ge(bank_done, i + 1)
                nc.scalar.activation(out_sb[:, h, cols(n)], acc[:, h, cols(n)], ACT.Identity,
                                     bias=bias[:, h:h + 1]).then_inc(act_bank_copied, 1)
                act.wait_ge(act_bank_copied, copied + 1)
                act.dma_start(out_t[h, :, cols(n)], out_sb[:, h, cols(n)]).then_inc(out_stored, DMA)

        @block.vector
        def _(dve):
            nc.vector.memset(zeros[:], 0.0).then_inc(zeros_ready, 1)

            def outer_product(g, j, slot):
                dve.wait_ge(zl_ready, steps_done(g, j - RING))
                nc.vector.tensor_tensor(z[:, j % RING, :], x0_rot[:, slot, :], x_rot[:, j, :],
                                        ALU.mult).then_inc(z_ready, 1)

            def z_rest(g, j):
                dve.wait_ge(zh_ready, steps_done(g, j))
                dve.wait_ge(chunk_multiplied, steps_done(g, j - RING))
                nc.vector.tensor_tensor(zl[:, j % RING, :], z[:, j % RING, :],
                                        zh[:, j % RING, :].bitcast(f32), ALU.subtract).then_inc(zl_ready, 1)

            def unit_product(u):
                j, first, last = UNITS[u]
                dve.wait_ge(unit_loaded[u], DMA * unit_loads[u])
                if slot_free(u):
                    dve.wait_ge(zl_ready, slot_free(u))
                nc.vector.tensor_tensor(z[:, j % RING, first:last], x0_rot[:, 0, first:last],
                                        x_rot[:, j, first:last], ALU.mult).then_inc(z_ready, 1)

            def unit_rest(u):
                j, first, last = UNITS[u]
                dve.wait_ge(zh_ready, u + 1)
                if slot_free(u):
                    dve.wait_ge(chunk_multiplied, slot_free(u))
                nc.vector.tensor_tensor(zl[:, j % RING, first:last], z[:, j % RING, first:last],
                                        zh[:, j % RING, first:last].bitcast(f32),
                                        ALU.subtract).then_inc(zl_ready, 1)

            def w_rest(j0, j1, slot):
                nc.vector.tensor_tensor(wl[:, slot, j0:j1], w_raw[:, slot, j0:j1],
                                        wh[:, slot, j0:j1].bitcast(f32), ALU.subtract).then_inc(wl_ready, 1)

            def next_wl(g, j):
                dve.wait_ge(wh_ready, splits_ready(g, j + 1))
                w_rest(0, PIECE, (j + 1) // PIECE % PIECES)

            def group(g, slot, x0_loads):
                for j in range(CHUNKS):
                    if j < CHUNKS - 1:
                        outer_product(g, j + 1, slot)
                    else:
                        dve.wait_ge(x0_loaded[1 - slot], DMA * x0_loads)
                        outer_product(g + 1, 0, 1 - slot)
                    z_rest(g, j)
                    if j % PIECE == PIECE - 1:
                        next_wl(g, j)

            for u in range(len(UNITS)):
                if u == 0:
                    unit_product(0)
                if u < len(FIRST_STEPS):
                    dve.wait_ge(wh_ready, u + 1)
                    w_rest(*FIRST_STEPS[u], 0)
                if u == 0:
                    unit_rest(0)
                    unit_product(1)
                    continue
                if u < len(UNITS) - 1:
                    unit_product(u + 1)
                else:
                    dve.wait_ge(x0_loaded[1], DMA)
                    outer_product(1, 0, 1)
                unit_rest(u)
                if u == SPLIT_SECOND:
                    dve.wait_ge(wh_ready, splits_ready(0, PIECE))
                    w_rest(0, PIECE, 1)
            next_wl(0, CHUNKS - 1)
            with dve.Fori(1, GROUPS - 1, 2) as g:
                group(g, 1, (g + 1) // 2)
                group(g + 1, 0, (g + 3) // 2)
            for j in range(CHUNKS):
                if j < CHUNKS - 1:
                    outer_product(GROUPS - 1, j + 1, 1)
                z_rest(GROUPS - 1, j)
                if j == PIECE - 1:
                    next_wl(GROUPS - 1, j)

            dve.wait_ge(bias_loaded, DMA)
            for i in dve_banks:
                h, n = banks[i]
                dve.wait_ge(bank_done, i + 1)
                nc.vector.tensor_scalar(out_sb[:, h, cols(n)], acc[:, h, cols(n)], bias[:, h:h + 1], None,
                                        ALU.add).then_inc(dve_bank_copied, 1)

        @block.tensor
        def _(pe):
            def product(w, zz, j, h, n, start=False, stop=False):
                wj = w[:, j // PIECE, j % PIECE, h * P:(h + 1) * P]
                return nc.tensor.matmul(acc[:, h, cols(n)], wj, zz[:, j % RING, cols(n)],
                                        start=start, stop=stop)

            def passes(j, blocks, count, start=False):
                pe.wait_ge(zh_ready, count)
                for n in blocks:
                    product(wl, zh, j, 0, n, start=start)
                for n in blocks:
                    product(wh, zh, j, 0, n)
                for n in blocks:
                    product(wl, zh, j, 1, n, start=start)
                for n in blocks:
                    product(wh, zh, j, 1, n)
                pe.wait_ge(zl_ready, count)
                for h in (1, 0):
                    for n in blocks:
                        done = product(wh, zl, j, h, n)
                done.then_inc(chunk_multiplied, 1)

            def chunk(g, j):
                if j % PIECE == 0:
                    pe.wait_ge(wl_ready, splits_ready(g, j))
                passes(j, range(BLOCKS), steps_done(g, j))

            pe.wait_ge(zeros_ready, 1)
            for _ in range(WARM_UP):
                nc.tensor.matmul(acc[:, HALVES - 1, cols(BLOCKS - 1)], zeros[:, 0:P], zeros[:],
                                 start=True, stop=True)

            for u, (j, first, last) in enumerate(UNITS):
                if u < len(FIRST_STEPS):
                    pe.wait_ge(wl_ready, u + 1)
                if u == SECOND_PIECE:
                    pe.wait_ge(wl_ready, splits_ready(0, PIECE))
                passes(j, range(first // NB, last // NB), u + 1, start=(j == 0))

            with pe.Fori(1, GROUPS - 1, 2) as g:
                for j in range(CHUNKS):
                    chunk(g, j)
                for j in range(CHUNKS):
                    chunk(g + 1, j)
            for j in range(CHUNKS - 1):
                chunk(GROUPS - 1, j)
            pe.wait_ge(zl_ready, steps_done(GROUPS - 1, CHUNKS - 1))
            for h, n in banks:
                product(wh, zh, CHUNKS - 1, h, n)
                product(wl, zh, CHUNKS - 1, h, n)
                product(wh, zl, CHUNKS - 1, h, n, stop=True).then_inc(bank_done, 1)


def kernel(r_x0, r_x, L0_rec_W, L0_rec_b):
    import numpy as np
    import concourse.bacc as bacc
    from concourse.bass_utils import run_bass_kernel_spmd

    x0_rows = np.ascontiguousarray(np.concatenate([r_x0.T, r_x0.T]))
    x_rows = np.ascontiguousarray(np.concatenate([r_x.T, r_x.T]))
    k = np.arange(P)
    f = (k[None, :] + CHUNKS * np.arange(GROUPS)[:, None]) % FIELD
    p = (k[None, :] + np.arange(CHUNKS)[:, None]) % H_PREV
    w_by_pair = np.ascontiguousarray(np.asarray(L0_rec_W).transpose(1, 2, 0))
    w_diag = w_by_pair[f[:, None, :], p[None, :, :]]
    w_pieces = np.ascontiguousarray(
        w_diag.reshape(GROUPS * PIECES, PIECE, P, H_NEXT).transpose(0, 2, 1, 3))
    bias_cols = np.ascontiguousarray(np.asarray(L0_rec_b).reshape(HALVES, P).T)

    nc = bacc.Bacc("TRN2", target_bir_lowering=False, num_devices=1)
    arrays = {"x0_rows": x0_rows, "x_rows": x_rows, "w_pieces": w_pieces, "bias_cols": bias_cols}
    args = [nc.dram_tensor(name, a.shape, mybir.dt.from_np(a.dtype), kind="ExternalInput").ap()
            for name, a in arrays.items()]
    out = nc.dram_tensor("out_t", (HALVES, P, BATCH), mybir.dt.float32, kind="ExternalOutput").ap()
    build(nc, *args, out)
    result = run_bass_kernel_spmd(nc, [arrays], core_ids=[0]).results[0]["out_t"]
    return np.ascontiguousarray(result.reshape(H_NEXT, BATCH).T)[:, :, None]
```
